# Optimizing a Trainium2 kernel written in Bass

```python
import numpy as np
import jax
import jax.numpy as jnp

def _softmax(x, axis=-1):
    return jax.nn.softmax(x, axis=axis)

def _gelu(x):
    return jax.nn.gelu(x, approximate=True)

def _silu(x):
    return jax.nn.silu(x)

def _sigmoid(x):
    return jax.nn.sigmoid(x)

def _layernorm(x, axis=-1, eps=1e-05):
    m = jnp.mean(x, axis=axis, keepdims=True)
    v = jnp.var(x, axis=axis, keepdims=True)
    return (x - m) / jnp.sqrt(v + eps)

def _scatter_add(tgt, idx, src, axis=0):
    return tgt.at[idx].add(src)

def _segment_sum(src, seg, n):
    return jax.ops.segment_sum(src, seg, n)
kernel_name = 'mk_adj_preln_d1_adj_r2_4c57ce'

def setup_inputs(seed: int=0):
    np.random.seed(seed)
    _w = jnp.asarray

    def _rec_inputs():
        import jax
        import jax.numpy as jnp
        _gk = jax.random.key(seed)
        x = -0.0005207 + 1.001 * jax.random.normal(jax.random.fold_in(_gk, 1), (4096, 128), jnp.float32)
        _a = jax.random.bernoulli(jax.random.fold_in(_gk, 2), 0.00390625, (4096, 4096))
        _a = jnp.logical_or(_a, jnp.eye(4096, dtype=bool))
        _af = _a.astype(jnp.float32)
        _af = _af * jax.random.uniform(jax.random.fold_in(_gk, 3), (4096, 4096), jnp.float32, 0.05, 1)
        adj = _af
        return (x, adj)
    x, adj = _rec_inputs()

    def _L0_gnn_setup():
        import jax, jax.numpy as jnp
        import numpy as np
        N = 4096
        D = 128
        L = 3

        def _cxin_conv(x, a, eps, W, b):
            ax = a @ x
            h = ax + (1.0 + eps[0]) * ax
            for i in range(L):
                h = jax.nn.relu(h @ W[i].T + b[i])
            return h
        key = jax.random.key(seed)
        ks = jax.random.split(key, 8)
        s = 1.0 / np.sqrt(D)
        return {'x1': jax.random.normal(ks[0], (N, D), jnp.float32), 'x2': jax.random.normal(ks[1], (N, D), jnp.float32), 'G1': jax.random.uniform(ks[2], (N, N), jnp.float32), 'G2': jax.random.uniform(ks[3], (N, N), jnp.float32), 'eps1': jnp.zeros((1,), jnp.float32), 'eps2': jnp.zeros((1,), jnp.float32), 'W1': jax.random.normal(ks[4], (L, D, D), jnp.float32) * s, 'b1': jnp.zeros((L, D), jnp.float32), 'W2': jax.random.normal(ks[5], (L, D, D), jnp.float32) * s, 'b2': jnp.zeros((L, D), jnp.float32), 'Wm': jax.random.normal(ks[6], (D, 2 * D), jnp.float32) * (1.0 / np.sqrt(2 * D)), 'bm': jnp.zeros((D,), jnp.float32)}
    _L0_gnn_all = _L0_gnn_setup()
    _L0_gnn_in = {k: v for k, v in _L0_gnn_all.items() if k in ('x2', 'eps1', 'eps2', 'W1', 'b1', 'W2', 'b2', 'Wm', 'bm')}
    del _L0_gnn_all
    return {'x': x, 'adj': adj, 'L0_gnn_x2': _L0_gnn_in['x2'], 'L0_gnn_eps1': _L0_gnn_in['eps1'], 'L0_gnn_eps2': _L0_gnn_in['eps2'], 'L0_gnn_W1': _L0_gnn_in['W1'], 'L0_gnn_b1': _L0_gnn_in['b1'], 'L0_gnn_W2': _L0_gnn_in['W2'], 'L0_gnn_b2': _L0_gnn_in['b2'], 'L0_gnn_Wm': _L0_gnn_in['Wm'], 'L0_gnn_bm': _L0_gnn_in['bm']}

def reference(x, adj, L0_gnn_x2, L0_gnn_eps1, L0_gnn_eps2, L0_gnn_W1, L0_gnn_b1, L0_gnn_W2, L0_gnn_b2, L0_gnn_Wm, L0_gnn_bm):
    import jax
    import jax.numpy as jnp

    def _L0_gnn_ref(x1, x2, G1, G2, eps1, eps2, W1, b1, W2, b2, Wm, bm):
        import jax, jax.numpy as jnp
        import numpy as np
        N = 4096
        D = 128
        L = 3

        def _cxin_conv(x, a, eps, W, b):
            ax = a @ x
            h = ax + (1.0 + eps[0]) * ax
            for i in range(L):
                h = jax.nn.relu(h @ W[i].T + b[i])
            return h
        out1 = _cxin_conv(x1, G1, eps1, W1, b1)
        out2 = _cxin_conv(x2, G2, eps2, W2, b2)
        merged = jnp.concatenate((out1, out2), axis=1)
        return merged @ Wm.T + bm
    h = jnp.maximum(_layernorm(x, axis=-1), 0.0)
    x = x + _L0_gnn_ref(h, L0_gnn_x2, adj, adj, L0_gnn_eps1, L0_gnn_eps2, L0_gnn_W1, L0_gnn_b1, L0_gnn_W2, L0_gnn_b2, L0_gnn_Wm, L0_gnn_bm)
    return x

_drawn_inputs = setup_inputs


def setup_inputs(seed=0):
    import zlib

    import numpy as np

    out = dict(_drawn_inputs(seed))
    spreads = {'L0_gnn_b1': (0.0, 0.301), 'L0_gnn_b2': (0.0, 0.302), 'L0_gnn_bm': (0.0, 0.1)}
    factors = {}
    for name, (base, spread) in spreads.items():
        noise = np.random.default_rng([zlib.crc32(name.encode()), seed]).standard_normal(out[name].shape)
        drawn = base * np.exp(spread * noise) if base else spread * noise
        out[name] = jnp.asarray(drawn.astype(out[name].dtype))
    for name, factor in factors.items():
        out[name] = (out[name] * factor).astype(out[name].dtype)
    return out
```

```python
from contextlib import ExitStack

import concourse.bass as bass
from concourse import mybir

F32 = mybir.dt.float32
F32R = mybir.dt.float32r
ALU = mybir.AluOpType
ACT = mybir.ActivationFunctionType

P = 128
ROWS = 512
KB_TILE = 4
RING = 4
STAGE = 2
LAYERS = 3
LN_EPS = 1e-5
X2, H = 0, 1


def gnn_kernel(nc, adj_tiles, x, x2, x_t, weights_t, biases, eps, out_t):
    GROUPS, TILES = adj_tiles.shape[0], adj_tiles.shape[1]
    KBS = TILES * KB_TILE
    TILE_COLS = KB_TILE * ROWS
    CHUNK = KB_TILE * P
    MATS = 2 * LAYERS + 2
    EVACS = 2 * (LAYERS + 1)
    assert x.shape == (P, KBS * P) and GROUPS * ROWS == x_t.shape[1] and TILES % RING == 0

    with ExitStack() as ctx:
        def sb(name, shape, dt=F32):
            return ctx.enter_context(nc.sbuf_tensor(name, shape, dt))

        def bank(name):
            return ctx.enter_context(nc.psum_tensor(name, [P, ROWS], F32))

        def sem(name):
            return ctx.enter_context(nc.semaphore(name))

        adj_raw = sb("adj_raw", [P, RING, TILE_COLS])
        adj_hi = sb("adj_hi", [P, RING, TILE_COLS], F32R)
        adj_lo = sb("adj_lo", [P, RING, TILE_COLS], F32R)
        feat_hi = sb("feat_hi", [P, 2, KBS * P], F32R)
        feat_lo = sb("feat_lo", [P, 2, KBS * P], F32R)
        x2_raw = sb("x2_raw", [P, STAGE, CHUNK])
        x_raw = sb("x_raw", [P, STAGE, CHUNK])
        x_norm = sb("x_norm", [P, CHUNK])
        stats = sb("stats", [P, KB_TILE, 6])
        mean_var = sb("mean_var", [P, KB_TILE, 2])
        variance = sb("variance", [P, KB_TILE])
        root = sb("root", [P, KB_TILE])
        root_inv = sb("root_inv", [P, KB_TILE])
        half_quot = sb("half_quot", [P, KB_TILE])
        std = sb("std", [P, KB_TILE])
        rstd = sb("rstd", [P, KB_TILE])
        w_raw = sb("w_raw", [P, MATS * P])
        w_hi = sb("w_hi", [P, MATS * P], F32R)
        w_lo = sb("w_lo", [P, MATS * P], F32R)
        bias = sb("bias", [P, 2 * LAYERS + 1])
        eps_sb = sb("eps_sb", [P, 2])
        agg_scale = sb("agg_scale", [P, 2])
        act_hi = sb("act_hi", [P, 2, ROWS], F32R)
        act_lo = sb("act_lo", [P, 2, ROWS], F32R)
        act_full = sb("act_full", [P, 2, ROWS])
        x_res = sb("x_res", [P, ROWS])
        y_sb = sb("y_sb", [P, ROWS])

        acc = [bank("acc_x2"), bank("acc_h")]
        layer_ps = [[bank(f"layer_ps{i}{b}") for b in (X2, H)] for i in range(2)]
        merge_ps = bank("merge_ps")

        adj_landed = [sem(f"adj_landed{s}") for s in range(RING)]
        x2_landed = [sem(f"x2_landed{s}") for s in range(STAGE)]
        x_landed = [sem(f"x_landed{s}") for s in range(STAGE)]
        w_landed = sem("w_landed")
        small_landed = sem("small_landed")
        adj_hi_done = sem("adj_hi_done")
        adj_lo_done = sem("adj_lo_done")
        tile_used = sem("tile_used")
        x2_hi_done = sem("x2_hi_done")
        x2_lo_done = sem("x2_lo_done")
        h_hi_done = sem("h_hi_done")
        h_lo_done = sem("h_lo_done")
        stats_done = sem("stats_done")
        moments_done = sem("moments_done")
        variance_done = sem("variance_done")
        root_done = sem("root_done")
        std_step = sem("std_step")
        norm_done = sem("norm_done")
        w_hi_done = sem("w_hi_done")
        w_lo_done = sem("w_lo_done")
        scale_part = sem("scale_part")
        scale_done = sem("scale_done")
        acc_done = [sem("acc_x2_done"), sem("acc_h_done")]
        layer_done = sem("layer_done")
        merge_done = sem("merge_done")
        act_hi_done = sem("act_hi_done")
        act_lo_done = sem("act_lo_done")
        act_full_done = sem("act_full_done")
        y_done = sem("y_done")
        res_in_y_out = sem("res_in_y_out")

        def mat(w, i):
            return w[:, i * P:(i + 1) * P]

        def layer_mat(i, b):
            return i if b == H else LAYERS + i

        def layer_bias(i, b):
            return bias[:, layer_mat(i, b):layer_mat(i, b) + 1]

        def chunk(feat, b, c):
            return feat[:, b, c * CHUNK:(c + 1) * CHUNK]

        def uses(g, t):
            return g * (TILES // RING) + t // RING + 1

        block = ctx.enter_context(nc.Block())

        @block.sync
        def _(sp):
            def load_tile(g, t, reused):
                if reused:
                    sp.wait_ge(adj_lo_done, g * TILES + (t - RING + 1))
                sp.dma_start(adj_raw[:, t % RING, :], adj_tiles[g, t]).then_inc(adj_landed[t % RING], 16)

            for c in range(TILES):
                if c >= STAGE:
                    sp.wait_ge(x2_hi_done, c - STAGE + 1)
                    sp.wait_ge(x2_lo_done, c - STAGE + 1)
                sp.dma_start(x2_raw[:, c % STAGE, :], x2[:, c * CHUNK:(c + 1) * CHUNK]).then_inc(x2_landed[c % STAGE], 16)
                load_tile(0, c, c >= RING)
                if c >= STAGE:
                    sp.wait_ge(norm_done, c - STAGE + 1)
                sp.dma_start(x_raw[:, c % STAGE, :], x[:, c * CHUNK:(c + 1) * CHUNK]).then_inc(x_landed[c % STAGE], 16)
            with sp.Fori(1, GROUPS) as g:
                for t in range(TILES):
                    load_tile(g, t, True)

        @block.gpsimd
        def _(pool):
            pool.dma_start(eps_sb[:, :], eps.to_broadcast([P, 2])).then_inc(small_landed, 16)
            pool.dma_start(bias[:, :], biases).then_inc(small_landed, 16)
            pool.dma_start(w_raw[:, :], weights_t).then_inc(w_landed, 16)
            for c in range(TILES):
                pool.wait_ge(x2_landed[c % STAGE], 16 * (c // STAGE + 1))
                pool.wait_ge(x2_hi_done, c + 1)
                pool.tensor_tensor(chunk(feat_lo, X2, c), x2_raw[:, c % STAGE, :], chunk(feat_hi, X2, c),
                                   ALU.subtract).then_inc(x2_lo_done, 1)

        @block.scalar
        def _(act):
            def split_tile(g, t, reused):
                act.wait_ge(adj_landed[t % RING], 16 * uses(g, t))
                if reused:
                    act.wait_ge(tile_used, g * TILES + (t - RING + 1))
                act.activation(adj_hi[:, t % RING, :], adj_raw[:, t % RING, :], ACT.Copy).then_inc(adj_hi_done, 1)

            def take_aggregate(g, b):
                act.wait_ge(acc_done[b], g + 1)
                act.activation(act_full[:, b, :], acc[b][:, :], ACT.Copy,
                               scale=agg_scale[:, b:b + 1]).then_inc(act_full_done, 1)

            def take_layer(g, i, b):
                act.wait_ge(layer_done, g * (2 * LAYERS) + (2 * i + b + 1))
                act.activation(act_full[:, b, :], layer_ps[i % 2][b][:, :], ACT.Relu,
                               bias=layer_bias(i, b)).then_inc(act_full_done, 1)

            def rows(g):
                return bass.ds(g * ROWS, ROWS)

            def load_residual(g):
                act.dma_start(x_res[:, :], x_t[:, rows(g)]).then_inc(res_in_y_out, 16)

            def store(g):
                act.wait_ge(y_done, g + 1)
                act.dma_start(out_t[:, rows(g)], y_sb[:, :]).then_inc(res_in_y_out, 16)

            load_residual(0)
            for c in range(TILES):
                act.wait_ge(x2_landed[c % STAGE], 16 * (c // STAGE + 1))
                act.activation(chunk(feat_hi, X2, c), x2_raw[:, c % STAGE, :], ACT.Copy).then_inc(x2_hi_done, 1)
                act.wait_ge(variance_done, c + 1)
                act.activation(root[:, :], variance[:, :], ACT.Sqrt).then_inc(root_done, 1)
                split_tile(0, c, c >= RING)
                act.wait_ge(norm_done, c + 1)
                act.activation(chunk(feat_hi, H, c), x_norm[:, :], ACT.Relu).then_inc(h_hi_done, 1)
                if c == 0:
                    act.wait_ge(small_landed, 32)
                    act.wait_ge(w_landed, 16)
                    act.activation(w_hi[:, :], w_raw[:, :], ACT.Copy).then_inc(w_hi_done, 1)
            act.wait_ge(scale_done, 2)
            with act.Fori(1, GROUPS) as g:
                for t in range(TILES):
                    split_tile(g, t, True)
                    if t == 1:
                        for b in (X2, H):
                            take_aggregate(g - 1, b)
                    if 3 <= t < 3 + LAYERS:
                        for b in (X2, H):
                            take_layer(g - 1, t - 3, b)
                store(g - 1)
                load_residual(g)
            for b in (X2, H):
                take_aggregate(GROUPS - 1, b)
            for i in range(LAYERS):
                for b in (X2, H):
                    take_layer(GROUPS - 1, i, b)
            store(GROUPS - 1)
            act.wait_ge(res_in_y_out, 16 * 2 * GROUPS)

        @block.vector
        def _(dve):
            def split_tile(g, t, reused):
                dve.wait_ge(adj_hi_done, g * TILES + (t + 1))
                if reused:
                    dve.wait_ge(tile_used, g * TILES + (t - RING + 1))
                dve.tensor_tensor(adj_lo[:, t % RING, :], adj_raw[:, t % RING, :], adj_hi[:, t % RING, :],
                                  ALU.subtract).then_inc(adj_lo_done, 1)

            def split_activations(g, i):
                for b in (X2, H):
                    dve.wait_ge(act_full_done, g * EVACS + (2 * i + b + 1))
                    dve.tensor_copy(act_hi[:, b, :], act_full[:, b, :]).then_inc(act_hi_done, 1)
                    dve.wait_ge(act_hi_done, g * EVACS + (2 * i + b + 1))
                    dve.tensor_tensor(act_lo[:, b, :], act_full[:, b, :], act_hi[:, b, :],
                                      ALU.subtract).then_inc(act_lo_done, 1)

            def residual(g):
                dve.wait_ge(merge_done, g + 1)
                dve.wait_ge(res_in_y_out, 16 * (2 * g + 1))
                dve.scalar_tensor_tensor(out=y_sb[:, :], in0=merge_ps[:, :], scalar=bias[:, 2 * LAYERS:2 * LAYERS + 1],
                                         in1=x_res[:, :], op0=ALU.add, op1=ALU.add).then_inc(y_done, 1)

            dve.wait_ge(small_landed, 32)
            for n, b in enumerate((H, X2)):
                dve.tensor_scalar(agg_scale[:, b:b + 1], eps_sb[:, n:n + 1], 1.0, 1.0, ALU.add,
                                  ALU.add).then_inc(scale_done, 1)
            for c in range(TILES):
                dve.wait_ge(x_landed[c % STAGE], 16 * (c // STAGE + 1))
                xc = x_raw[:, c % STAGE, :]
                for k in range(KB_TILE):
                    dve.bn_stats(stats[:, k, :], xc[:, k * P:(k + 1) * P]).then_inc(stats_done, 1)
                dve.wait_ge(stats_done, KB_TILE * (c + 1))
                for k in range(KB_TILE):
                    dve.bn_aggr(mean_var[:, k, :], stats[:, k, :]).then_inc(moments_done, 1)
                dve.wait_ge(moments_done, KB_TILE * (c + 1))
                dve.tensor_scalar(variance[:, :], mean_var[:, :, 1], LN_EPS, None, ALU.add).then_inc(variance_done, 1)
                split_tile(0, c, c >= RING)
                dve.wait_ge(root_done, c + 1)
                dve.reciprocal(root_inv[:, :], root[:, :]).then_inc(std_step, 1)
                dve.wait_ge(std_step, 4 * c + 1)
                dve.scalar_tensor_tensor(out=half_quot[:, :], in0=variance[:, :], scalar=0.5, in1=root_inv[:, :],
                                         op0=ALU.mult, op1=ALU.mult).then_inc(std_step, 1)
                dve.wait_ge(std_step, 4 * c + 2)
                dve.scalar_tensor_tensor(out=std[:, :], in0=root[:, :], scalar=0.5, in1=half_quot[:, :],
                                         op0=ALU.mult, op1=ALU.add).then_inc(std_step, 1)
                dve.wait_ge(std_step, 4 * c + 3)
                dve.reciprocal(rstd[:, :], std[:, :]).then_inc(std_step, 1)
                dve.wait_ge(std_step, 4 * c + 4)
                for k in range(KB_TILE):
                    last = dve.tensor_scalar(x_norm[:, k * P:(k + 1) * P], xc[:, k * P:(k + 1) * P], mean_var[:, k, 0:1],
                                             rstd[:, k:k + 1], ALU.subtract, ALU.mult)
                last.then_inc(norm_done, 1)
                dve.wait_ge(norm_done, c + 1)
                dve.wait_ge(h_hi_done, c + 1)
                dve.scalar_tensor_tensor(out=chunk(feat_lo, H, c), in0=x_norm[:, :], scalar=0.0, in1=chunk(feat_hi, H, c),
                                         op0=ALU.max, op1=ALU.subtract).then_inc(h_lo_done, 1)
                if c == 0:
                    dve.wait_ge(w_landed, 16)
                    dve.wait_ge(w_hi_done, 1)
                    dve.tensor_tensor(w_lo[:, :], w_raw[:, :], w_hi[:, :], ALU.subtract).then_inc(w_lo_done, 1)
            with dve.Fori(1, GROUPS) as g:
                for t in range(TILES):
                    split_tile(g, t, True)
                    if t == 1:
                        split_activations(g - 1, 0)
                    if 3 <= t < 3 + LAYERS:
                        split_activations(g - 1, t - 2)
                    if t == 3 + LAYERS:
                        residual(g - 1)
            for i in range(LAYERS + 1):
                split_activations(GROUPS - 1, i)
            residual(GROUPS - 1)

        @block.tensor
        def _(pe):
            def aggregate(g, t, prologue):
                pe.wait_ge(adj_hi_done, g * TILES + (t + 1))
                for b in (X2, H):
                    if prologue:
                        pe.wait_ge((x2_hi_done, h_hi_done)[b], t + 1)
                        pe.wait_ge((x2_lo_done, h_lo_done)[b], t + 1)
                    elif t == 0:
                        pe.wait_ge(act_full_done, (g - 1) * EVACS + (b + 1))
                    for lo_tile in (False, True):
                        if lo_tile and b == X2:
                            pe.wait_ge(adj_lo_done, g * TILES + (t + 1))
                        for k in range(KB_TILE):
                            rows = (adj_lo if lo_tile else adj_hi)[:, t % RING, k * ROWS:(k + 1) * ROWS]
                            kb = t * KB_TILE + k
                            for feat in (feat_hi,) if lo_tile else (feat_hi, feat_lo):
                                mm = pe.matmul(acc[b][:, :], feat[:, b, kb * P:(kb + 1) * P], rows,
                                               start=(kb == 0 and not lo_tile and feat is feat_hi),
                                               stop=(kb == KBS - 1 and lo_tile))
                    if t == TILES - 1:
                        mm.then_inc(acc_done[b], 1)
                    if b == H and t < TILES - 1:
                        mm.then_inc(tile_used, 1)
                if t == TILES - 1:
                    pe.wait_ge(acc_done[H], g + 1)
                    pe.nop().then_inc(tile_used, 1)

            def product(out, terms):
                parts = [(mat(w, i), a[:, b, :]) for w, a in ((w_hi, act_hi), (w_lo, act_hi), (w_hi, act_lo))
                         for i, b in terms]
                for n, (w, a) in enumerate(parts):
                    mm = pe.matmul(out[:, :], w, a, start=(n == 0), stop=(n == len(parts) - 1))
                return mm

            def layer(g, i):
                for b in (X2, H):
                    pe.wait_ge(act_lo_done, g * EVACS + (2 * i + b + 1))
                    product(layer_ps[i % 2][b], [(layer_mat(i, b), b)]).then_inc(layer_done, 1)

            def merge(g):
                pe.wait_ge(act_lo_done, g * EVACS + EVACS)
                product(merge_ps, [(2 * LAYERS + 1, X2), (2 * LAYERS, H)]).then_inc(merge_done, 1)

            for t in range(TILES):
                aggregate(0, t, True)
            pe.wait_ge(w_hi_done, 1)
            pe.wait_ge(w_lo_done, 1)
            with pe.Fori(1, GROUPS) as g:
                for t in range(TILES):
                    aggregate(g, t, False)
                    if 1 <= t < 1 + LAYERS:
                        layer(g - 1, t - 1)
                    if t == 1 + LAYERS:
                        merge(g - 1)
            for i in range(LAYERS):
                layer(GROUPS - 1, i)
            merge(GROUPS - 1)


def kernel(x, adj, L0_gnn_x2, L0_gnn_eps1, L0_gnn_eps2, L0_gnn_W1, L0_gnn_b1, L0_gnn_W2, L0_gnn_b2, L0_gnn_Wm,
           L0_gnn_bm):
    import numpy as np
    import concourse.bacc as bacc
    from concourse.bass_utils import run_bass_kernel_spmd

    x, adj, x2 = np.asarray(x), np.asarray(adj), np.asarray(L0_gnn_x2)
    n, d = x.shape
    groups, tiles = n // ROWS, n // (P * KB_TILE)
    adj_tiles = np.ascontiguousarray(
        adj.reshape(groups, ROWS, P, tiles, KB_TILE).transpose(0, 3, 2, 4, 1)).reshape(groups, tiles, P, KB_TILE * ROWS)
    w1, w2, wm = np.asarray(L0_gnn_W1), np.asarray(L0_gnn_W2), np.asarray(L0_gnn_Wm)
    weights_t = np.concatenate([w.T for w in w1] + [w.T for w in w2] + [wm[:, :d].T, wm[:, d:].T], axis=1)
    biases = np.concatenate([np.asarray(L0_gnn_b1).T, np.asarray(L0_gnn_b2).T, np.asarray(L0_gnn_bm)[:, None]], axis=1)
    eps = np.concatenate([np.asarray(L0_gnn_eps1), np.asarray(L0_gnn_eps2)])[None, :]
    arrays = {
        "adj_tiles": adj_tiles,
        "x": np.ascontiguousarray(x).reshape(P, -1),
        "x2": np.ascontiguousarray(x2).reshape(P, -1),
        "x_t": np.ascontiguousarray(x.T),
        "weights_t": np.ascontiguousarray(weights_t),
        "biases": np.ascontiguousarray(biases),
        "eps": np.ascontiguousarray(eps),
    }
    nc = bacc.Bacc("TRN2", target_bir_lowering=False, num_devices=1)
    args = [nc.dram_tensor(name, a.shape, mybir.dt.from_np(a.dtype), kind="ExternalInput").ap()
            for name, a in arrays.items()]
    args.append(nc.dram_tensor("y_t", (d, n), F32, kind="ExternalOutput").ap())
    gnn_kernel(nc, *args)
    r = run_bass_kernel_spmd(nc, [arrays], core_ids=[0])
    return np.ascontiguousarray(r.results[0]["y_t"].T)
```

```python
from contextlib import ExitStack

import concourse.bass as bass
from concourse import mybir

F32 = mybir.dt.float32
F32R = mybir.dt.float32r
ALU = mybir.AluOpType
ACT = mybir.ActivationFunctionType

P = 128
ROWS = 512
KB_TILE = 4
RING = 4
STAGE = 4
LAYERS = 3
LN_EPS = 1e-5
POOL_FROM = 1
WARM = 8
X2, H = 0, 1


def gnn_kernel(nc, adj_tiles, x, x2, x_t, weights_t, biases, eps, out_t):
    GROUPS, TILES = adj_tiles.shape[0], adj_tiles.shape[1]
    KBS = TILES * KB_TILE
    TILE_COLS = KB_TILE * ROWS
    CHUNK = KB_TILE * P
    MATS = 2 * LAYERS + 2
    PIECES = {0: KB_TILE, 1: 2, 2: 2}
    EARLY = [(t, p) for t, n in PIECES.items() for p in range(n - 1)]
    EVACS = 2 * (LAYERS + 1)
    assert x.shape == (P, KBS * P) and GROUPS * ROWS == x_t.shape[1] and TILES % RING == 0

    with ExitStack() as ctx:
        def sb(name, shape, dt=F32):
            return ctx.enter_context(nc.sbuf_tensor(name, shape, dt))

        def bank(name):
            return ctx.enter_context(nc.psum_tensor(name, [P, ROWS], F32))

        def sem(name):
            return ctx.enter_context(nc.semaphore(name))

        adj_raw = sb("adj_raw", [P, RING, TILE_COLS])
        adj_hi = sb("adj_hi", [P, RING, TILE_COLS], F32R)
        adj_lo = sb("adj_lo", [P, RING, TILE_COLS], F32R)
        feat_hi = sb("feat_hi", [P, 2, KBS * P], F32R)
        feat_lo = sb("feat_lo", [P, 2, KBS * P], F32R)
        x2_raw = sb("x2_raw", [P, STAGE, CHUNK])
        x_raw = sb("x_raw", [P, STAGE, CHUNK])
        x_norm = sb("x_norm", [P, CHUNK])
        stats = sb("stats", [P, KB_TILE, 6])
        mean_var = sb("mean_var", [P, 2, KB_TILE, 2])
        variance = sb("variance", [P, KB_TILE])
        root = sb("root", [P, KB_TILE])
        root_inv = sb("root_inv", [P, KB_TILE])
        half_quot = sb("half_quot", [P, KB_TILE])
        std = sb("std", [P, KB_TILE])
        rstd = sb("rstd", [P, KB_TILE])
        w_raw = sb("w_raw", [P, MATS * P])
        w_hi = sb("w_hi", [P, MATS * P], F32R)
        w_lo = sb("w_lo", [P, MATS * P], F32R)
        pool_scratch = sb("pool_scratch", [P, 3])
        warm = sb("warm", [P, ROWS], mybir.dt.bfloat16)
        act_scratch = sb("act_scratch", [P, 2])
        bias = sb("bias", [P, 2 * LAYERS + 1])
        eps_sb = sb("eps_sb", [P, 2])
        agg_scale = sb("agg_scale", [P, 2])
        act_hi = sb("act_hi", [P, 2, ROWS], F32R)
        act_lo = sb("act_lo", [P, 2, ROWS], F32R)
        act_full = sb("act_full", [P, 2, ROWS])
        x_cent = act_full[:, 0, 0:CHUNK]
        x_res = sb("x_res", [P, ROWS])
        y_sb = sb("y_sb", [P, ROWS])

        acc = [bank("acc_x2"), bank("acc_h")]
        layer_ps = [[bank(f"layer_ps{i}{b}") for b in (X2, H)] for i in range(2)]
        merge_ps = bank("merge_ps")

        HALVES = (slice(0, ROWS // 2), slice(ROWS // 2, ROWS))
        last_merge_ps = [merge_ps[:, HALVES[0]], layer_ps[1][X2][:, HALVES[1]]]

        adj_landed = [sem(f"adj_landed{s}") for s in range(RING)]
        early_landed = [sem(f"early_landed{n}") for n in range(len(EARLY))]
        x2_landed = [sem(f"x2_landed{s}") for s in range(STAGE)]
        x_landed = [sem(f"x_landed{s}") for s in range(STAGE)]
        pool_scratch_set = sem("pool_scratch_set")
        act_scratch_set = sem("act_scratch_set")
        warm_set = sem("warm_set")
        w_landed = sem("w_landed")
        small_landed = sem("small_landed")
        adj_hi_done = sem("adj_hi_done")
        adj_lo_done = sem("adj_lo_done")
        early_hi_done = sem("early_hi_done")
        early_lo_done = sem("early_lo_done")
        tile_used = sem("tile_used")
        x2_hi_done = sem("x2_hi_done")
        x2_lo_done = sem("x2_lo_done")
        h_hi_done = sem("h_hi_done")
        h_lo_done = sem("h_lo_done")
        stats_done = sem("stats_done")
        moments_done = sem("moments_done")
        variance_done = sem("variance_done")
        root_done = sem("root_done")
        std_step = sem("std_step")
        cent_done = sem("cent_done")
        norm_done = sem("norm_done")
        w_hi_done = sem("w_hi_done")
        w_lo_done = sem("w_lo_done")
        scale_done = sem("scale_done")
        acc_x2_done = sem("acc_x2_done")
        layer_done = sem("layer_done")
        merge_done = sem("merge_done")
        act_hi_done = sem("act_hi_done")
        act_lo_done = sem("act_lo_done")
        act_full_done = sem("act_full_done")
        last_layer_done = [sem("last_layer_done_x2"), sem("last_layer_done_h")]
        last_full_done = sem("last_full_done")
        y_done = sem("y_done")
        res_in_y_out = sem("res_in_y_out")

        def mat(w, i):
            return w[:, i * P:(i + 1) * P]

        def layer_mat(i, b):
            return i if b == H else LAYERS + i

        def layer_bias(i, b):
            return bias[:, layer_mat(i, b):layer_mat(i, b) + 1]

        def chunk(feat, b, c):
            return feat[:, b, c * CHUNK:(c + 1) * CHUNK]

        def uses(g, t):
            return g * (TILES // RING) + t // RING + 1

        def pieces(t):
            n = PIECES.get(t, 1)
            return [(p * KB_TILE // n, KB_TILE // n, EARLY.index((t, p)) if p < n - 1 else None) for p in range(n)]

        block = ctx.enter_context(nc.Block())

        @block.sync
        def _(sp):
            def load_tile(g, t):
                sp.wait_ge(adj_lo_done, g * TILES + (t - RING + 1))
                sp.dma_start(adj_raw[:, t % RING, :], adj_tiles[g, t]).then_inc(adj_landed[t % RING], 16)

            def load_x2(c):
                if c >= STAGE:
                    sp.wait_ge(x2_hi_done, c - STAGE + 1)
                    sp.wait_ge(x2_lo_done, c - STAGE + 1)
                sp.dma_start(x2_raw[:, c % STAGE, :], x2[:, c * CHUNK:(c + 1) * CHUNK]).then_inc(x2_landed[c % STAGE], 16)

            def load_x(c):
                if c >= STAGE:
                    sp.wait_ge(norm_done, c - STAGE + 1)
                sp.dma_start(x_raw[:, c % STAGE, :], x[:, c * CHUNK:(c + 1) * CHUNK]).then_inc(x_landed[c % STAGE], 16)

            load_x2(0)
            for t in range(TILES):
                for k, n, early in pieces(t):
                    if t >= RING:
                        sp.wait_ge(adj_lo_done, t - RING + 1)
                    cols = slice(k * ROWS, (k + n) * ROWS)
                    sp.dma_start(adj_raw[:, t % RING, cols], adj_tiles[0, t, :, cols]).then_inc(
                        adj_landed[t % RING] if early is None else early_landed[early], 16)
                    if t == 0 and k == 0:
                        load_x(0)
                if t == RING - 1:
                    sp.dma_start(eps_sb[:, :], eps.to_broadcast([P, 2])).then_inc(small_landed, 16)
                    sp.dma_start(bias[:, :], biases).then_inc(small_landed, 16)
                    sp.dma_start(w_raw[:, :], weights_t).then_inc(w_landed, 16)
                if t + 1 < TILES:
                    load_x(t + 1)
                    load_x2(t + 1)
            with sp.Fori(1, GROUPS) as g:
                for t in range(TILES):
                    load_tile(g, t)

        @block.gpsimd
        def _(pool):
            pool.memset(pool_scratch[:, :], 0.0).then_inc(pool_scratch_set, 1)
            pool.wait_ge(pool_scratch_set, 1)
            pool.tensor_tensor(pool_scratch[:, 0:1], pool_scratch[:, 1:2], pool_scratch[:, 2:3], ALU.subtract)
            for c in range(POOL_FROM, TILES):
                pool.wait_ge(x2_landed[c % STAGE], 16 * (c // STAGE + 1))
                pool.wait_ge(x2_hi_done, c + 1)
                pool.tensor_tensor(chunk(feat_lo, X2, c), x2_raw[:, c % STAGE, :], chunk(feat_hi, X2, c),
                                   ALU.subtract).then_inc(x2_lo_done, 1)
                per_node = lambda v: v.to_broadcast([P, KB_TILE, P])
                nodes = lambda v: v.rearrange("p (k d) -> p k d", k=KB_TILE)
                pool.wait_ge(x_landed[c % STAGE], 16 * (c // STAGE + 1))
                pool.wait_ge(moments_done, KB_TILE * (c + 1))
                if c > POOL_FROM:
                    pool.wait_ge(norm_done, c)
                pool.tensor_tensor(nodes(x_cent), nodes(x_raw[:, c % STAGE, :]),
                                   per_node(mean_var[:, c % 2, :, 0:1]), ALU.subtract).then_inc(cent_done, 1)
                pool.wait_ge(cent_done, c - POOL_FROM + 1)
                pool.wait_ge(std_step, 4 * c + 4)
                pool.tensor_tensor(nodes(x_norm[:, :]), nodes(x_cent), per_node(rstd[:, :].rearrange("p (k o) -> p k o", o=1)),
                                   ALU.mult).then_inc(norm_done, 1)

        @block.scalar
        def _(act):
            def split_tile(g, t):
                act.wait_ge(adj_landed[t % RING], 16 * uses(g, t))
                act.wait_ge(tile_used, g * TILES + (t - RING + 1))
                act.activation(adj_hi[:, t % RING, :], adj_raw[:, t % RING, :], ACT.Copy).then_inc(adj_hi_done, 1)

            def split_piece(t, k, n, early):
                if early is None:
                    act.wait_ge(adj_landed[t % RING], 16 * uses(0, t))
                else:
                    act.wait_ge(early_landed[early], 16)
                if t >= RING:
                    act.wait_ge(tile_used, t - RING + 1)
                cols = slice(k * ROWS, (k + n) * ROWS)
                act.activation(adj_hi[:, t % RING, cols], adj_raw[:, t % RING, cols], ACT.Copy).then_inc(
                    adj_hi_done if early is None else early_hi_done, 1)

            def split_x2(c):
                act.wait_ge(x2_landed[c % STAGE], 16 * (c // STAGE + 1))
                act.activation(chunk(feat_hi, X2, c), x2_raw[:, c % STAGE, :], ACT.Copy).then_inc(x2_hi_done, 1)

            def root_of_variance(c):
                act.wait_ge(variance_done, c + 1)
                act.activation(root[:, :], variance[:, :], ACT.Sqrt).then_inc(root_done, 1)

            def split_h(c):
                act.wait_ge(norm_done, c + 1)
                act.activation(chunk(feat_hi, H, c), x_norm[:, :], ACT.Relu).then_inc(h_hi_done, 1)

            def take_aggregate(g, b):
                if b == X2:
                    act.wait_ge(acc_x2_done, g + 1)
                else:
                    act.wait_ge(tile_used, (g + 1) * TILES)
                act.activation(act_full[:, b, :], acc[b][:, :], ACT.Copy,
                               scale=agg_scale[:, b:b + 1]).then_inc(act_full_done, 1)

            def take_layer(g, i, b):
                act.wait_ge(layer_done, g * (2 * LAYERS) + (2 * i + b + 1))
                act.activation(act_full[:, b, :], layer_ps[i % 2][b][:, :], ACT.Relu,
                               bias=layer_bias(i, b)).then_inc(act_full_done, 1)

            def rows(g):
                return bass.ds(g * ROWS, ROWS)

            def load_residual(g):
                act.dma_start(x_res[:, :], x_t[:, rows(g)]).then_inc(res_in_y_out, 16)

            def store(g):
                act.wait_ge(y_done, g + 1)
                act.dma_start(out_t[:, rows(g)], y_sb[:, :]).then_inc(res_in_y_out, 16)

            act.wait_ge(act_scratch_set, 1)
            act.activation(act_scratch[:, 0:1], act_scratch[:, 1:2], ACT.Sqrt)
            split_x2(0)
            for t in range(TILES):
                for n, piece in enumerate(pieces(t)):
                    split_piece(t, *piece)
                    if t < 2 and n == 1 - t:
                        root_of_variance(t)
                if t + 1 < TILES:
                    split_x2(t + 1)
                split_h(t)
                if 1 <= t < TILES - 1:
                    root_of_variance(t + 1)
                if t == TILES // 2:
                    act.wait_ge(w_landed, 16)
                    act.activation(w_hi[:, :], w_raw[:, :], ACT.Copy).then_inc(w_hi_done, 1)
            load_residual(0)
            act.wait_ge(small_landed, 32)
            act.wait_ge(scale_done, 2)
            with act.Fori(1, GROUPS) as g:
                for t in range(TILES):
                    split_tile(g, t)
                    if t == 1:
                        for b in (X2, H):
                            take_aggregate(g - 1, b)
                    if 3 <= t < 3 + LAYERS:
                        for b in (X2, H):
                            take_layer(g - 1, t - 3, b)
                store(g - 1)
                load_residual(g)
            take_aggregate(GROUPS - 1, X2)
            for i in range(LAYERS):
                act.wait_ge(last_layer_done[X2], i + 1)
                act.activation(act_full[:, X2, :], layer_ps[i % 2][X2][:, :], ACT.Relu,
                               bias=layer_bias(i, X2)).then_inc(act_full_done, 1)
            for half, cols in enumerate(HALVES):
                act.wait_ge(y_done, GROUPS + half)
                act.dma_start(out_t[:, (GROUPS - 1) * ROWS + cols.start:(GROUPS - 1) * ROWS + cols.stop],
                              y_sb[:, cols]).then_inc(res_in_y_out, 16)
            act.wait_ge(res_in_y_out, 16 * (2 * GROUPS + 1))

        @block.vector
        def _(dve):
            def split_tile(g, t):
                dve.wait_ge(adj_hi_done, g * TILES + (t + 1))
                dve.wait_ge(tile_used, g * TILES + (t - RING + 1))
                dve.tensor_tensor(adj_lo[:, t % RING, :], adj_raw[:, t % RING, :], adj_hi[:, t % RING, :],
                                  ALU.subtract).then_inc(adj_lo_done, 1)

            def split_activations(g, i):
                for b in (X2, H):
                    dve.wait_ge(act_full_done, g * EVACS + (2 * i + b + 1))
                    dve.tensor_copy(act_hi[:, b, :], act_full[:, b, :]).then_inc(act_hi_done, 1)
                    dve.wait_ge(act_hi_done, g * EVACS + (2 * i + b + 1))
                    dve.tensor_tensor(act_lo[:, b, :], act_full[:, b, :], act_hi[:, b, :],
                                      ALU.subtract).then_inc(act_lo_done, 1)

            def residual(g):
                dve.wait_ge(merge_done, g + 1)
                dve.wait_ge(res_in_y_out, 16 * (2 * g + 1))
                dve.scalar_tensor_tensor(out=y_sb[:, :], in0=merge_ps[:, :], scalar=bias[:, 2 * LAYERS:2 * LAYERS + 1],
                                         in1=x_res[:, :], op0=ALU.add, op1=ALU.add).then_inc(y_done, 1)

            def split_piece(t, k, n, early):
                if early is None:
                    dve.wait_ge(adj_hi_done, t + 1)
                else:
                    dve.wait_ge(early_hi_done, early + 1)
                if t >= RING:
                    dve.wait_ge(tile_used, t - RING + 1)
                cols = slice(k * ROWS, (k + n) * ROWS)
                dve.tensor_tensor(adj_lo[:, t % RING, cols], adj_raw[:, t % RING, cols], adj_hi[:, t % RING, cols],
                                  ALU.subtract).then_inc(adj_lo_done if early is None else early_lo_done, 1)

            def split_x2(c):
                dve.wait_ge(x2_hi_done, c + 1)
                dve.tensor_tensor(chunk(feat_lo, X2, c), x2_raw[:, c % STAGE, :], chunk(feat_hi, X2, c),
                                  ALU.subtract).then_inc(x2_lo_done, 1)

            def node_stats(c, k):
                if k == 0:
                    dve.wait_ge(x_landed[c % STAGE], 16 * (c // STAGE + 1))
                dve.bn_stats(stats[:, k, :], x_raw[:, c % STAGE, k * P:(k + 1) * P]).then_inc(stats_done, 1)

            def variances(c):
                for k in range(KB_TILE):
                    dve.wait_ge(stats_done, KB_TILE * c + k + 1)
                    dve.bn_aggr(mean_var[:, c % 2, k, :], stats[:, k, :]).then_inc(moments_done, 1)
                dve.wait_ge(moments_done, KB_TILE * (c + 1))
                dve.tensor_scalar(variance[:, :], mean_var[:, c % 2, :, 1], LN_EPS, None, ALU.add).then_inc(variance_done, 1)

            def deviations(c, next_stats):
                def between(k):
                    if next_stats:
                        node_stats(c + 1, k)

                dve.wait_ge(root_done, c + 1)
                dve.reciprocal(root_inv[:, :], root[:, :]).then_inc(std_step, 1)
                between(0)
                dve.wait_ge(std_step, 4 * c + 1)
                dve.scalar_tensor_tensor(out=half_quot[:, :], in0=variance[:, :], scalar=0.5, in1=root_inv[:, :],
                                         op0=ALU.mult, op1=ALU.mult).then_inc(std_step, 1)
                between(1)
                dve.wait_ge(std_step, 4 * c + 2)
                dve.scalar_tensor_tensor(out=std[:, :], in0=root[:, :], scalar=0.5, in1=half_quot[:, :],
                                         op0=ALU.mult, op1=ALU.add).then_inc(std_step, 1)
                between(2)
                dve.wait_ge(std_step, 4 * c + 3)
                dve.reciprocal(rstd[:, :], std[:, :]).then_inc(std_step, 1)
                between(3)
                dve.wait_ge(std_step, 4 * c + 4)
                if c < POOL_FROM:
                    for k in range(KB_TILE):
                        cols = slice(k * P, (k + 1) * P)
                        last = dve.tensor_scalar(x_norm[:, cols], x_raw[:, c % STAGE, cols],
                                                 mean_var[:, c % 2, k, 0:1], rstd[:, k:k + 1], ALU.subtract, ALU.mult)
                    last.then_inc(norm_done, 1)
                if next_stats:
                    variances(c + 1)

            def split_h(c):
                dve.wait_ge(norm_done, c + 1)
                dve.wait_ge(h_hi_done, c + 1)
                dve.scalar_tensor_tensor(out=chunk(feat_lo, H, c), in0=x_norm[:, :], scalar=0.0, in1=chunk(feat_hi, H, c),
                                         op0=ALU.max, op1=ALU.subtract).then_inc(h_lo_done, 1)

            dve.memset(act_scratch[:, :], 1.0).then_inc(act_scratch_set, 1)
            dve.memset(warm[:, :].bitcast(F32), 0.0).then_inc(warm_set, 1)
            split_x2(0)
            first, second, *rest = pieces(0)
            split_piece(0, *first)
            for k in range(KB_TILE):
                node_stats(0, k)
            variances(0)
            split_piece(0, *second)
            deviations(0, False)
            for piece in rest:
                split_piece(0, *piece)
            split_h(0)
            for k in range(KB_TILE):
                node_stats(1, k)
            variances(1)
            for t in range(1, TILES):
                if t < POOL_FROM:
                    split_x2(t)
                before = pieces(t)[:-1]
                for piece in before:
                    split_piece(t, *piece)
                deviations(t, t + 1 < TILES)
                split_piece(t, *pieces(t)[-1])
                split_h(t)
                if t == TILES // 2:
                    dve.wait_ge(w_hi_done, 1)
                    dve.tensor_tensor(w_lo[:, :], w_raw[:, :], w_hi[:, :], ALU.subtract).then_inc(w_lo_done, 1)
                    dve.wait_ge(small_landed, 32)
                    for n, b in enumerate((H, X2)):
                        dve.tensor_scalar(agg_scale[:, b:b + 1], eps_sb[:, n:n + 1], 1.0, 1.0, ALU.add,
                                          ALU.add).then_inc(scale_done, 1)
            with dve.Fori(1, GROUPS) as g:
                for t in range(TILES):
                    split_tile(g, t)
                    if t == 1:
                        split_activations(g - 1, 0)
                    if 3 <= t < 3 + LAYERS:
                        split_activations(g - 1, t - 2)
                    if t == 3 + LAYERS:
                        residual(g - 1)
            dve.wait_ge(tile_used, GROUPS * TILES)
            dve.tensor_scalar(act_full[:, H, :], acc[H][:, :], agg_scale[:, H:H + 1], None,
                              ALU.mult).then_inc(last_full_done, 1)
            for i in range(LAYERS):
                dve.wait_ge(last_layer_done[H], i + 1)
                dve.tensor_scalar(act_full[:, H, :], layer_ps[i % 2][H][:, :], layer_bias(i, H), 0.0,
                                  ALU.add, ALU.max).then_inc(last_full_done, 1)
            dve.wait_ge(res_in_y_out, 16 * (2 * GROUPS - 1))
            for half, cols in enumerate(HALVES):
                dve.wait_ge(merge_done, GROUPS + half)
                dve.scalar_tensor_tensor(out=y_sb[:, cols], in0=last_merge_ps[half],
                                         scalar=bias[:, 2 * LAYERS:2 * LAYERS + 1], in1=x_res[:, cols],
                                         op0=ALU.add, op1=ALU.add).then_inc(y_done, 1)

        @block.tensor
        def _(pe):
            def add_blocks(b, t, k, n, lo_tile):
                for kb in range(t * KB_TILE + k, t * KB_TILE + k + n):
                    col = kb % KB_TILE * ROWS
                    rows = (adj_lo if lo_tile else adj_hi)[:, t % RING, col:col + ROWS]
                    for feat in (feat_hi,) if lo_tile else (feat_hi, feat_lo):
                        mm = pe.matmul(acc[b][:, :], feat[:, b, kb * P:(kb + 1) * P], rows,
                                       start=(kb == 0 and not lo_tile and feat is feat_hi),
                                       stop=(kb == KBS - 1 and lo_tile))
                return mm

            def aggregate_first(t):
                pe.wait_ge(x2_hi_done, t + 1)
                pe.wait_ge(x2_lo_done, t + 1)
                for k, n, early in pieces(t):
                    pe.wait_ge(*((adj_hi_done, t + 1) if early is None else (early_hi_done, early + 1)))
                    add_blocks(X2, t, k, n, False)
                    pe.wait_ge(*((adj_lo_done, t + 1) if early is None else (early_lo_done, early + 1)))
                    mm = add_blocks(X2, t, k, n, True)
                if t == TILES - 1:
                    mm.then_inc(acc_x2_done, 1)
                pe.wait_ge(h_hi_done, t + 1)
                pe.wait_ge(h_lo_done, t + 1)
                add_blocks(H, t, 0, KB_TILE, False)
                add_blocks(H, t, 0, KB_TILE, True).then_inc(tile_used, 1)

            def aggregate(g, t):
                pe.wait_ge(adj_hi_done, g * TILES + (t + 1))
                if t == 0:
                    pe.wait_ge(act_full_done, (g - 1) * EVACS + 1)
                add_blocks(X2, t, 0, KB_TILE, False)
                pe.wait_ge(adj_lo_done, g * TILES + (t + 1))
                mm = add_blocks(X2, t, 0, KB_TILE, True)
                if t == TILES - 1:
                    mm.then_inc(acc_x2_done, 1)
                if t == 0:
                    pe.wait_ge(act_full_done, (g - 1) * EVACS + 2)
                add_blocks(H, t, 0, KB_TILE, False)
                add_blocks(H, t, 0, KB_TILE, True).then_inc(tile_used, 1)

            def product(out, terms):
                parts = [(mat(w, i), a[:, b, :]) for w, a in ((w_hi, act_hi), (w_lo, act_hi), (w_hi, act_lo))
                         for i, b in terms]
                for n, (w, a) in enumerate(parts):
                    mm = pe.matmul(out[:, :], w, a, start=(n == 0), stop=(n == len(parts) - 1))
                return mm

            def layer(g, i):
                for b in (X2, H):
                    pe.wait_ge(act_lo_done, g * EVACS + (2 * i + b + 1))
                    product(layer_ps[i % 2][b], [(layer_mat(i, b), b)]).then_inc(layer_done, 1)

            def merge(g):
                pe.wait_ge(act_lo_done, g * EVACS + EVACS)
                product(merge_ps, [(2 * LAYERS + 1, X2), (2 * LAYERS, H)]).then_inc(merge_done, 1)

            pe.wait_ge(warm_set, 1)
            for _ in range(WARM):
                pe.matmul(merge_ps[:, :], warm[:, 0:P], warm[:, :], start=True, stop=True)
            for t in range(TILES):
                aggregate_first(t)
            pe.wait_ge(w_lo_done, 1)
            with nc.Fori(1, GROUPS, engines=(mybir.EngineType.PE,), hint_back_edge=True) as g:
                for t in range(TILES):
                    aggregate(g, t)
                    if 1 <= t < 1 + LAYERS:
                        layer(g - 1, t - 1)
                    if t == 1 + LAYERS:
                        merge(g - 1)
            def last_operands_ready(i):
                return ((act_full_done, (GROUPS - 1) * EVACS + i + 1), (last_full_done, i + 1))

            for i in range(LAYERS):
                for b in (X2, H):
                    pe.wait_ge(*last_operands_ready(i)[b])
                    pe.matmul(layer_ps[i % 2][b][:, :], mat(w_raw, layer_mat(i, b)), act_full[:, b, :],
                              start=True, stop=True).then_inc(last_layer_done[b], 1)
            for b in (X2, H):
                pe.wait_ge(*last_operands_ready(LAYERS)[b])
                for half, cols in enumerate(HALVES):
                    mm = pe.matmul(last_merge_ps[half], mat(w_raw, 2 * LAYERS + (b == X2)), act_full[:, b, cols],
                                   start=(b == X2), stop=(b == H))
                    if b == H:
                        mm.then_inc(merge_done, 1)


def kernel(x, adj, L0_gnn_x2, L0_gnn_eps1, L0_gnn_eps2, L0_gnn_W1, L0_gnn_b1, L0_gnn_W2, L0_gnn_b2, L0_gnn_Wm,
           L0_gnn_bm):
    import numpy as np
    import concourse.bacc as bacc
    from concourse.bass_utils import run_bass_kernel_spmd

    x, adj, x2 = np.asarray(x), np.asarray(adj), np.asarray(L0_gnn_x2)
    n, d = x.shape
    groups, tiles = n // ROWS, n // (P * KB_TILE)
    adj_tiles = np.ascontiguousarray(
        adj.reshape(groups, ROWS, P, tiles, KB_TILE).transpose(0, 3, 2, 4, 1)).reshape(groups, tiles, P, KB_TILE * ROWS)
    w1, w2, wm = np.asarray(L0_gnn_W1), np.asarray(L0_gnn_W2), np.asarray(L0_gnn_Wm)
    weights_t = np.concatenate([w.T for w in w1] + [w.T for w in w2] + [wm[:, :d].T, wm[:, d:].T], axis=1)
    biases = np.concatenate([np.asarray(L0_gnn_b1).T, np.asarray(L0_gnn_b2).T, np.asarray(L0_gnn_bm)[:, None]], axis=1)
    eps = np.concatenate([np.asarray(L0_gnn_eps1), np.asarray(L0_gnn_eps2)])[None, :]
    arrays = {
        "adj_tiles": adj_tiles,
        "x": np.ascontiguousarray(x).reshape(P, -1),
        "x2": np.ascontiguousarray(x2).reshape(P, -1),
        "x_t": np.ascontiguousarray(x.T),
        "weights_t": np.ascontiguousarray(weights_t),
        "biases": np.ascontiguousarray(biases),
        "eps": np.ascontiguousarray(eps),
    }
    nc = bacc.Bacc("TRN2", target_bir_lowering=False, num_devices=1)
    args = [nc.dram_tensor(name, a.shape, mybir.dt.from_np(a.dtype), kind="ExternalInput").ap()
            for name, a in arrays.items()]
    args.append(nc.dram_tensor("y_t", (d, n), F32, kind="ExternalOutput").ap())
    gnn_kernel(nc, *args)
    r = run_bass_kernel_spmd(nc, [arrays], core_ids=[0])
    return np.ascontiguousarray(r.results[0]["y_t"].T)
```
